# Optimizing a Trainium2 kernel written in Bass

```python
import numpy as np
import jax
import jax.numpy as jnp

def _softmax(x, axis=-1):
    return jax.nn.softmax(x, axis=axis)
def _gelu(x):
    return jax.nn.gelu(x, approximate=True)
def _silu(x):
    return jax.nn.silu(x)
def _sigmoid(x):
    return jax.nn.sigmoid(x)
def _layernorm(x, axis=-1, eps=1e-5):
    m = jnp.mean(x, axis=axis, keepdims=True)
    v = jnp.var(x, axis=axis, keepdims=True)
    return (x - m) / jnp.sqrt(v + eps)
def _scatter_add(tgt, idx, src, axis=0):
    return tgt.at[idx].add(src)
def _segment_sum(src, seg, n):
    return jax.ops.segment_sum(src, seg, n)

kernel_name = 'mk_conv_preact_d2_conv_nchw64_ce596e'

def setup_inputs(seed: int = 0):
    np.random.seed(seed)
    _w = jnp.asarray
    def _rec_inputs():
        import jax
        import jax.numpy as jnp
        _gk = jax.random.key(seed)
        x = 1.508e-05 + 1 * jax.random.normal(jax.random.fold_in(_gk, 1), (16, 64, 256, 256), jnp.float32)
        return x
    x = _rec_inputs()
    def _L0_conv_setup():
        import jax, jax.numpy as jnp
        import numpy as np
        from jax import lax
        EPS = 1e-08

        def _depthwise_sobel(x):
            c = x.shape[1]
            kx = jnp.array([[-1.0, 0.0, 1.0], [-2.0, 0.0, 2.0], [-1.0, 0.0, 1.0]], dtype=x.dtype)
            ky = jnp.array([[1.0, 2.0, 1.0], [0.0, 0.0, 0.0], [-1.0, -2.0, -1.0]], dtype=x.dtype)
            wx = jnp.tile(kx[None, None], (c, 1, 1, 1))
            wy = jnp.tile(ky[None, None], (c, 1, 1, 1))
            dn = lax.conv_dimension_numbers(x.shape, wx.shape, ('NCHW', 'OIHW', 'NCHW'))
            gx = lax.conv_general_dilated(x, wx, window_strides=(1, 1), padding='SAME', dimension_numbers=dn, feature_group_count=c)
            gy = lax.conv_general_dilated(x, wy, window_strides=(1, 1), padding='SAME', dimension_numbers=dn, feature_group_count=c)
            return jnp.sqrt(gx * gx + gy * gy + EPS)
        key = jax.random.key(seed)
        x = jax.random.normal(key, (16, 64, 256, 256), dtype=jnp.float32)
        return {'x': x}
    _L0_conv_all = _L0_conv_setup()
    _L0_conv_in = {k: v for k, v in _L0_conv_all.items() if k in ()}
    del _L0_conv_all

    def _L1_conv_setup():
        import jax, jax.numpy as jnp
        import numpy as np
        NC = 64
        B, H, W = (32, 128, 128)
        key = jax.random.key(seed)
        kx, = jax.random.split(key, 1)
        x = jax.random.normal(kx, (B, NC, H, W), dtype=jnp.float32)
        exp_param = jnp.eye(NC, dtype=jnp.float32)[:, :, None, None]
        bias = jnp.zeros((NC, 1, 1), dtype=jnp.float32)
        return {'x': x, 'exp_param': exp_param, 'bias': bias}
    _L1_conv_all = _L1_conv_setup()
    _L1_conv_in = {k: v for k, v in _L1_conv_all.items() if k in ('exp_param', 'bias', )}
    del _L1_conv_all

    return {
        "x": x,
        "L1_conv_exp_param": _L1_conv_in["exp_param"],
        "L1_conv_bias": _L1_conv_in["bias"],
    }

def reference(x, L1_conv_exp_param, L1_conv_bias):
    import jax
    import jax.numpy as jnp
    def _L0_conv_ref(x):
        import jax, jax.numpy as jnp
        import numpy as np
        from jax import lax
        EPS = 1e-08

        def _depthwise_sobel(x):
            c = x.shape[1]
            kx = jnp.array([[-1.0, 0.0, 1.0], [-2.0, 0.0, 2.0], [-1.0, 0.0, 1.0]], dtype=x.dtype)
            ky = jnp.array([[1.0, 2.0, 1.0], [0.0, 0.0, 0.0], [-1.0, -2.0, -1.0]], dtype=x.dtype)
            wx = jnp.tile(kx[None, None], (c, 1, 1, 1))
            wy = jnp.tile(ky[None, None], (c, 1, 1, 1))
            dn = lax.conv_dimension_numbers(x.shape, wx.shape, ('NCHW', 'OIHW', 'NCHW'))
            gx = lax.conv_general_dilated(x, wx, window_strides=(1, 1), padding='SAME', dimension_numbers=dn, feature_group_count=c)
            gy = lax.conv_general_dilated(x, wy, window_strides=(1, 1), padding='SAME', dimension_numbers=dn, feature_group_count=c)
            return jnp.sqrt(gx * gx + gy * gy + EPS)
        return _depthwise_sobel(x)

    def _L1_conv_ref(x, exp_param, bias):
        import jax, jax.numpy as jnp
        import numpy as np
        NC = 64
        B, H, W = (32, 128, 128)
        xr = jax.nn.relu(x) + 0.1
        E = exp_param[:, :, 0, 0]
        logx = jnp.log(xr)
        out = jnp.exp(jnp.einsum('bihw,ij->bjhw', logx, E)) + bias
        return out

    def _gn(v, G=32, eps=1e-5):
        B_, C_, H_, W_ = v.shape
        g = v.reshape(B_, G, C_ // G, H_, W_)
        m = jnp.mean(g, axis=(2, 3, 4), keepdims=True)
        s = jnp.var(g, axis=(2, 3, 4), keepdims=True)
        return ((g - m) / jnp.sqrt(s + eps)).reshape(v.shape)

    def _ln_c(v, eps=1e-6):
        m = jnp.mean(v, axis=1, keepdims=True)
        s = jnp.var(v, axis=1, keepdims=True)
        return (v - m) / jnp.sqrt(s + eps)

    def _ln_t(v, eps=1e-5):
        m = jnp.mean(v, axis=-1, keepdims=True)
        s = jnp.var(v, axis=-1, keepdims=True)
        return (v - m) / jnp.sqrt(s + eps)

    def _to_tokens(v):
        B_, C_, H_, W_ = v.shape
        return v.reshape(B_, C_, H_ * W_).transpose(0, 2, 1)
    def _from_tokens(t, like):
        B_, C_, H_, W_ = like.shape
        return t.transpose(0, 2, 1).reshape(B_, C_, H_, W_)

    x = x + _L0_conv_ref(_gn(x))
    x = x + _L1_conv_ref(_gn(x), L1_conv_exp_param, L1_conv_bias)
    return x


_drawn_inputs = setup_inputs


def setup_inputs(seed=0):
    import zlib

    import numpy as np

    out = dict(_drawn_inputs(seed))
    spreads = {'L1_conv_bias': (0.0, 0.419)}
    factors = {}
    for name, (base, spread) in spreads.items():
        noise = np.random.default_rng([zlib.crc32(name.encode()), seed]).standard_normal(out[name].shape)
        drawn = base * np.exp(spread * noise) if base else spread * noise
        out[name] = jnp.asarray(drawn.astype(out[name].dtype))
    for name, factor in factors.items():
        out[name] = (out[name] * factor).astype(out[name].dtype)
    return out
```

```python
from contextlib import ExitStack

import concourse.bass as bass
from concourse import mybir

F32 = mybir.dt.float32
ALU = mybir.AluOpType
ACT = mybir.ActivationFunctionType

P = 128
ROWS = 8
BANK = 512
STAT = 6
GN_EPS = 1e-5
SOBEL_EPS = 1e-8
LOG_SHIFT = 0.1


def build(nc, x, exp_param, bias, eye, neg_eye, group_mean, out):
    IMAGES, C, H, W = x.shape
    HALF = H // 2
    N = ROWS * W
    CH = HALF // ROWS
    PAIRS = CH // 2
    BN = N // BANK
    BROWS = BANK // W
    LAG = 6
    assert 2 * C == P and HALF % (2 * ROWS) == 0 and BANK % W == 0 and LAG % 2 == 0

    x_dram = x.rearrange("b c (h r) w -> b h c (r w)", h=2)
    out_dram = out.rearrange("b c (h r) w -> b h c (r w)", h=2)

    with ExitStack() as ctx:
        def sb(name, shape):
            return ctx.enter_context(nc.sbuf_tensor(name, shape, F32))

        def ps(name):
            return ctx.enter_context(nc.psum_tensor(name, [P, N], F32))

        def sem(name):
            return ctx.enter_context(nc.semaphore(name))

        image = sb("image", [P, (HALF + 2) * W])
        pair_sum = sb("pair_sum", [P, ROWS, W + 2])
        top_pair = sb("top_pair", [P, 1, W + 2])
        box = sb("box", [P, 2, ROWS, W + 1])
        work = [sb(f"work{i}", [P, N]) for i in range(4)]
        zeros = sb("zeros", [P, W])
        plus = sb("plus", [P, P])
        minus = sb("minus", [P, P])
        grp = sb("grp", [P, P])
        mix = sb("mix", [P, P])
        bias_sb = sb("bias_sb", [P, 1])
        eps_sobel = sb("eps_sobel", [P, 1])
        eps_gn = sb("eps_gn", [P, 1])
        shift = sb("shift", [P, 1])
        bn = sb("bn", [P, CH * BN * STAT])
        aggr = sb("aggr", [P, 2])
        gx = sb("gx", [P, 2])
        sx = sb("sx", [P, 4])
        y_sum = sb("y_sum", [P, CH])
        y_sq = sb("y_sq", [P, CH])
        ry = sb("ry", [P, 2])
        gy = sb("gy", [P, 2])
        sy = sb("sy", [P, 5])
        psum = [ps("psum0"), ps("psum1")]

        squares, q_sq, junk = work[0:2], work[2], work[3]
        logs, exps = work[0:2], work[2:4]

        const_in = sem("const_in")
        const_set = sem("const_set")
        mix_zero = sem("mix_zero")
        halo_in = sem("halo_in")
        chunk_in = [sem("chunk_in0"), sem("chunk_in1")]
        chunk_out = [sem("chunk_out0"), sem("chunk_out1")]
        bn_done = sem("bn_done")
        x_stat = sem("x_stat")
        x_scaled = sem("x_scaled")
        x_grouped = sem("x_grouped")
        padded = sem("padded")
        pairs_done = sem("pairs_done")
        top_done = sem("top_done")
        box_done = sem("box_done")
        carry_used = sem("carry_used")
        p_ready = sem("p_ready")
        q_ready = sem("q_ready")
        p_squared = sem("p_squared")
        q_squared = sem("q_squared")
        summed = sem("summed")
        rooted = sem("rooted")
        y_ready = sem("y_ready")
        y_squared = sem("y_squared")
        y_stat = sem("y_stat")
        y_grouped = sem("y_grouped")
        y_std = sem("y_std")
        clamped = sem("clamped")
        logged = sem("logged")
        mixed = sem("mixed")
        exped = sem("exped")
        final = sem("final")

        PADS = 4
        X_STATS = 5
        Y_STATS = 7

        def rows(k, n=N, ahead=0):
            return image[:, bass.ds(k * N + (1 + ahead) * W, n)]

        def rows3(k, ahead=0):
            return rows(k, ahead=ahead).rearrange("p (r w) -> p r w", w=W)

        block = ctx.enter_context(nc.Block())

        @block.sync
        def _(sp):
            def load(n, k, u):
                for h in range(2):
                    sp.dma_start(image[h * C:(h + 1) * C, bass.ds(k * N + W, N)],
                                 x_dram[bass.ds(n, 1), h, :, bass.ds(k * N, N)].rearrange("b c f -> (b c) f")
                                 ).then_inc(chunk_in[u], 16)

            def halos(n):
                sp.dma_start(image[C:P, 0:W],
                             x_dram[bass.ds(n, 1), 0, :, (HALF - 1) * W:HALF * W].rearrange("b c f -> (b c) f")
                             ).then_inc(halo_in, 16)
                sp.dma_start(image[0:C, (HALF + 1) * W:(HALF + 2) * W],
                             x_dram[bass.ds(n, 1), 1, :, 0:W].rearrange("b c f -> (b c) f")
                             ).then_inc(halo_in, 16)

            def store(n, k, u):
                for h in range(2):
                    sp.dma_start(out_dram[bass.ds(n, 1), h, :, bass.ds(k * N, N)].rearrange("b c f -> (b c) f"),
                                 image[h * C:(h + 1) * C, bass.ds(k * N + W, N)]).then_inc(chunk_out[u], 16)

            halos(0)
            for k in range(CH):
                if k >= 2:
                    sp.wait_ge(chunk_in[k % 2], 32 * (k // 2))
                load(0, k, k % 2)
            for dst, src in ((plus[:], eye), (minus[:], neg_eye), (grp[:], group_mean)):
                sp.dma_start(dst, src).then_inc(const_in, 16)
            sp.wait_ge(mix_zero, 1)
            for h in range(2):
                sp.dma_start(mix[h * C:(h + 1) * C, h * C:(h + 1) * C],
                             exp_param.rearrange("i j a b -> i (j a b)")).then_inc(const_in, 16)
                sp.dma_start(bias_sb[h * C:(h + 1) * C, :],
                             bias.rearrange("c a b -> c (a b)")).then_inc(const_in, 16)

            def stores(n, more):
                def refill(k, pair, u):
                    stored = n * (32 * PAIRS) + 32 * pair + 32
                    landed = (n * CH + k) * 16 + (32 * PAIRS - 16 * u)
                    sp.wait_ge(chunk_out[u], stored)
                    if more:
                        sp.wait_ge(chunk_in[u], landed)
                        load(n + 1, k, u)

                if more:
                    sp.wait_ge(box_done, n * CH + CH)
                    halos(n + 1)
                for k in range(2):
                    sp.wait_ge(final, n * CH + k + 1)
                    store(n, k, k)
                with sp.Fori(0, PAIRS - 1) as t:
                    for u in range(2):
                        if more:
                            refill(2 * t + u, t, u)
                        sp.wait_ge(final, n * CH + 2 * t + u + 3)
                        store(n, 2 * t + u + 2, u)
                for u in range(2):
                    refill(CH - 2 + u, PAIRS - 1, u)

            with sp.Fori(0, IMAGES - 1) as n:
                stores(n, True)
            stores(IMAGES - 1, False)

        @block.gpsimd
        def _(pool):
            nc.gpsimd.memset(mix[:], 0.0).then_inc(mix_zero, 1)
            for t, v in ((zeros, 0.0), (eps_sobel, SOBEL_EPS), (eps_gn, GN_EPS), (shift, LOG_SHIFT)):
                nc.gpsimd.memset(t[:], v).then_inc(const_set, 1)

        @block.vector
        def _(dve):
            v = nc.vector

            def x_chunk_stats(k, u, arrived, index=None):
                dve.wait_ge(chunk_in[u], arrived)
                for b in range(BN):
                    i = v.bn_stats(bn[:, bass.ds(k * (BN * STAT) + b * STAT, STAT)], image[:, bass.ds(k * N + W + b * BANK, BANK)])
                i.then_inc(bn_done, 1)

            def x_stats(n):
                s = n * X_STATS
                dve.wait_ge(bn_done, n * CH + CH)
                v.memset(sx[:, 2:3], 0.0)
                v.bn_aggr(aggr[:], bn[:]).then_inc(x_stat, 1)
                dve.wait_ge(x_stat, s + 1)
                v.scalar_tensor_tensor(out=aggr[:, 1:2], in0=aggr[:, 0:1], scalar=aggr[:, 0:1], in1=aggr[:, 1:2],
                                       op0=ALU.mult, op1=ALU.add).then_inc(x_stat, 1)
                dve.wait_ge(x_grouped, n + 1)
                v.tensor_copy(gx[:], psum[0][:, 0:2]).then_inc(x_stat, 1)
                dve.wait_ge(x_stat, s + 3)
                v.tensor_scalar(sx[:, 0:1], gx[:, 0:1], 2.0, None, ALU.mult)
                v.tensor_scalar(sx[:, 1:2], gx[:, 0:1], -1.0, None, ALU.mult)
                v.tensor_scalar(sx[:, 2:3], gx[:, 0:1], gx[:, 0:1], None, ALU.mult).then_inc(x_stat, 1)
                dve.wait_ge(x_stat, s + 4)
                v.tensor_tensor(sx[:, 2:3], gx[:, 1:2], sx[:, 2:3], ALU.subtract).then_inc(x_stat, 1)

            def x_scale(n):
                dve.wait_ge(x_stat, n * X_STATS + 5)
                v.tensor_scalar(sx[:, 3:4], sx[:, 2:3], GN_EPS, 0.5, ALU.add, ALU.mult).then_inc(x_scaled, 1)
                dve.wait_ge(x_scaled, 2 * n + 1)
                v.reciprocal(sx[:, 3:4], sx[:, 3:4]).then_inc(x_scaled, 1)

            def top(n):
                dve.wait_ge(halo_in, n * 32 + 32)
                dve.wait_ge(padded, n * PADS + PADS)
                v.tensor_tensor(top_pair[:, 0, 1:W + 1], image[:, 0:W], image[:, W:2 * W], ALU.add).then_inc(top_done, 1)
                dve.wait_ge(top_done, 2 * n + 1)
                v.tensor_tensor(box[:, 1, ROWS - 1, :], top_pair[:, 0, 0:W + 1], top_pair[:, 0, 1:W + 2],
                                ALU.add).then_inc(top_done, 1)

            def pair_rows(n, k):
                dve.wait_ge(box_done, n * CH + k) if not (isinstance(k, int) and k == 0) else None
                v.tensor_tensor(pair_sum[:, :, 1:W + 1], rows3(k), rows3(k, ahead=1), ALU.add).then_inc(pairs_done, 1)

            def boxes(n, k, u):
                dve.wait_ge(pairs_done, n * CH + k + 1)
                if not (isinstance(k, int) and k == 0):
                    dve.wait_ge(carry_used, n * CH + k)
                v.tensor_tensor(box[:, u], pair_sum[:, :, 0:W + 1], pair_sum[:, :, 1:W + 2], ALU.add).then_inc(box_done, 1)

            def add_squares(n, k, u):
                dve.wait_ge(q_squared, n * CH + k + 1)
                v.tensor_tensor(squares[u][:], squares[u][:], q_sq[:], ALU.add).then_inc(summed, 1)

            def add_root(n, k, u):
                dve.wait_ge(rooted, n * CH + k + 1)
                v.scalar_tensor_tensor(out=rows(k), in0=squares[u][:], scalar=1.0, in1=rows(k), op0=ALU.mult,
                                       op1=ALU.add, accum_out=y_sum[:, bass.ds(k, 1)]).then_inc(y_ready, 1)

            def phase_a(n):
                x_stats(n)
                x_scale(n)
                top(n)
                pair_rows(n, 0)
                boxes(n, 0, 0)
                pair_rows(n, 1)
                boxes(n, 1, 1)
                add_squares(n, 0, 0)
                with dve.Fori(0, PAIRS - 1) as t:
                    for u in range(2):
                        k = 2 * t + 2 + u
                        pair_rows(n, k)
                        add_squares(n, k - 1, 1 - u)
                        boxes(n, k, u)
                        add_root(n, k - 2, u)
                add_squares(n, CH - 1, 1)
                add_root(n, CH - 2, 0)
                add_root(n, CH - 1, 1)

            def y_stats(n):
                s = n * Y_STATS
                dve.wait_ge(y_ready, n * CH + CH)
                v.reduce_sum(ry[:, 0:1], y_sum[:], mybir.AxisListType.X)
                dve.wait_ge(y_squared, n * CH + CH)
                v.reduce_sum(ry[:, 1:2], y_sq[:], mybir.AxisListType.X).then_inc(y_stat, 1)
                dve.wait_ge(y_grouped, n + 1)
                v.tensor_scalar(gy[:], psum[0][:, 0:2], 1.0 / (HALF * W), None, ALU.mult).then_inc(y_stat, 1)
                dve.wait_ge(y_stat, s + 2)
                v.tensor_tensor(sy[:, 0:1], gy[:, 0:1], gx[:, 0:1], ALU.subtract).then_inc(y_stat, 1)
                dve.wait_ge(y_stat, s + 3)
                v.tensor_tensor(sy[:, 1:2], sy[:, 0:1], sy[:, 0:1], ALU.mult).then_inc(y_stat, 1)
                dve.wait_ge(y_stat, s + 4)
                v.tensor_tensor(sy[:, 2:3], gy[:, 1:2], sy[:, 1:2], ALU.subtract).then_inc(y_stat, 1)
                dve.wait_ge(y_std, n + 1)
                v.reciprocal(sy[:, 4:5], sy[:, 3:4]).then_inc(y_stat, 1)
                dve.wait_ge(y_stat, s + 6)
                v.tensor_copy(sy[:, 0:1], sy[:, 4:5]).then_inc(y_stat, 1)

            def clamp(n, k, u):
                if not (isinstance(k, int) and k < 2):
                    dve.wait_ge(mixed, n * CH + k - 1)
                v.tensor_scalar(logs[u][:], rows(k), gy[:, 0:1], gy[:, 0:1], ALU.max, ALU.subtract).then_inc(clamped, 1)

            def finish(n, k, u):
                dve.wait_ge(exped, n * CH + k + 1)
                v.scalar_tensor_tensor(out=rows(k), in0=exps[u][:], scalar=bias_sb[:, 0:1], in1=rows(k),
                                       op0=ALU.add, op1=ALU.add).then_inc(final, 1)

            def next_stats(n, k, pair, u):
                x_chunk_stats(k, u, n * (32 * PAIRS) + 32 * pair + 32 * PAIRS + 32)

            def phase_b(n, more):
                y_stats(n)
                for k in range(LAG):
                    clamp(n, k, k % 2)
                    if k >= 2:
                        finish(n, k - 2, k % 2)
                with dve.Fori(0, (CH - LAG) // 2) as t:
                    for u in range(2):
                        k = 2 * t + LAG + u
                        clamp(n, k, u)
                        finish(n, k - 2, u)
                        if more:
                            next_stats(n, k - LAG, t, u)
                finish(n, CH - 2, 0)
                finish(n, CH - 1, 1)
                if more:
                    for k in range(CH - LAG, CH):
                        next_stats(n, k, k // 2, k % 2)

            for k in range(CH):
                x_chunk_stats(k, k % 2, 32 * (k // 2 + 1))
            dve.wait_ge(const_in, 16 * 7)
            with dve.Fori(0, IMAGES - 1) as n:
                phase_a(n)
                phase_b(n, True)
            phase_a(IMAGES - 1)
            phase_b(IMAGES - 1, False)

        @block.scalar
        def _(act):
            a = nc.scalar

            def pad(n):
                act.wait_ge(x_stat, n * X_STATS + 4)
                a.activation(image[0:C, 0:W], zeros[0:C, :], ACT.Identity, bias=gx[0:C, 0:1]).then_inc(padded, 1)
                a.activation(image[C:P, (HALF + 1) * W:(HALF + 2) * W], zeros[C:P, :], ACT.Identity,
                             bias=gx[C:P, 0:1]).then_inc(padded, 1)
                for tile, r in ((pair_sum, ROWS), (top_pair, 1)):
                    a.activation(tile[:, :, 0:W + 2:W + 1], zeros[:, 0:2 * r].rearrange("p (r c) -> p r c", c=2),
                                 ACT.Identity, bias=sx[:, 0:1]).then_inc(padded, 1)

            def square(n, k, u):
                act.wait_ge(p_ready, n * CH + k + 1)
                if not (isinstance(k, int) and k < 2):
                    act.wait_ge(y_ready, n * CH + k - 1)
                a.activation(squares[u][:], psum[0][:], ACT.Square).then_inc(p_squared, 1)
                act.wait_ge(q_ready, n * CH + k + 1)
                if not (isinstance(k, int) and k == 0):
                    act.wait_ge(summed, n * CH + k)
                a.activation(q_sq[:], psum[1][:], ACT.Square).then_inc(q_squared, 1)

            def root(n, k, u):
                act.wait_ge(summed, n * CH + k + 1)
                a.activation(squares[u][:], squares[u][:], ACT.Sqrt, bias=eps_sobel[:, 0:1],
                             scale=sx[:, 3:4]).then_inc(rooted, 1)

            def square_y(n, k):
                act.wait_ge(y_ready, n * CH + k + 1)
                if not (isinstance(k, int) and k == 0):
                    act.wait_ge(y_squared, n * CH + k)
                a.activation(junk[:], rows(k), ACT.Square, bias=sx[:, 1:2],
                             accum_out=y_sq[:, bass.ds(k, 1)]).then_inc(y_squared, 1)

            def phase_a(n):
                a.preload_act_table_set("sqrt_and_others")
                pad(n)
                square(n, 0, 0)
                act.wait_ge(x_scaled, 2 * n + 2)
                root(n, 0, 0)
                square(n, 1, 1)
                with act.Fori(0, PAIRS - 1) as t:
                    for u in range(2):
                        k = 2 * t + 2 + u
                        root(n, k - 1, 1 - u)
                        square(n, k, u)
                        square_y(n, k - 2)
                root(n, CH - 1, 1)
                square_y(n, CH - 2)
                square_y(n, CH - 1)
                act.wait_ge(y_stat, n * Y_STATS + 5)
                a.activation(sy[:, 3:4], sy[:, 2:3], ACT.Sqrt, bias=eps_gn[:, 0:1]).then_inc(y_std, 1)

            def log(n, k, u):
                act.wait_ge(clamped, n * CH + k + 1)
                a.activation(logs[u][:], logs[u][:], ACT.Ln, bias=shift[:, 0:1], scale=sy[:, 4:5]).then_inc(logged, 1)

            def exp(n, k, u):
                act.wait_ge(mixed, n * CH + k + 1)
                if not (isinstance(k, int) and k < 2):
                    act.wait_ge(final, n * CH + k - 1)
                a.activation(exps[u][:], psum[u][:], ACT.Exp).then_inc(exped, 1)

            def phase_b(n):
                a.preload_act_table_set("natural_log_exp_and_others")
                act.wait_ge(y_stat, n * Y_STATS + 6)
                log(n, 0, 0)
                log(n, 1, 1)
                exp(n, 0, 0)
                with act.Fori(0, PAIRS - 1) as t:
                    for u in range(2):
                        k = 2 * t + 2 + u
                        log(n, k, u)
                        exp(n, k - 1, 1 - u)
                exp(n, CH - 1, 1)

            act.wait_ge(const_set, 4)
            with act.Fori(0, IMAGES) as n:
                phase_a(n)
                phase_b(n)

        @block.tensor
        def _(pe):
            def difference(n, k, u, bank, which):
                dst = psum[which][:, bank * BANK:(bank + 1) * BANK]
                r = bank * BROWS
                low = slice(0, W) if which == 0 else slice(1, W + 1)
                up = slice(1, W + 1) if which == 0 else slice(0, W)
                w_low, w_up = (minus, plus) if which == 0 else (plus, minus)
                nc.tensor.matmul(dst, w_low[:], box[:, u, r:r + BROWS, low], start=True, stop=False)
                if bank == 0:
                    nc.tensor.matmul(dst[:, 0:W], w_up[:], box[:, 1 - u, ROWS - 1, up], start=False, stop=False)
                    return nc.tensor.matmul(dst[:, W:BANK], w_up[:], box[:, u, 0:BROWS - 1, up], start=False, stop=True)
                return nc.tensor.matmul(dst, w_up[:], box[:, u, r - 1:r - 1 + BROWS, up], start=False, stop=True)

            def differences(n, k, u):
                first = isinstance(k, int) and k == 0
                pe.wait_ge(box_done, n * CH + k + 1)
                if first:
                    pe.wait_ge(top_done, 2 * n + 2)
                else:
                    pe.wait_ge(p_squared, n * CH + k)
                for bank in reversed(range(BN)):
                    i = difference(n, k, u, bank, 0)
                i.then_inc(p_ready, 1)
                if not first:
                    pe.wait_ge(q_squared, n * CH + k)
                for bank in range(BN):
                    i = difference(n, k, u, bank, 1)
                    if bank == 0:
                        i.then_inc(carry_used, 1)
                i.then_inc(q_ready, 1)

            def group(n, src, ready, value, signal):
                pe.wait_ge(ready, value)
                nc.tensor.matmul(psum[0][:, 0:2], grp[:], src[:], start=True, stop=True).then_inc(signal, 1)

            def mix_channels(n, k, u):
                pe.wait_ge(logged, n * CH + k + 1)
                if not (isinstance(k, int) and k < 2):
                    pe.wait_ge(exped, n * CH + k - 1)
                for b in range(BN):
                    i = nc.tensor.matmul(psum[u][:, b * BANK:(b + 1) * BANK], mix[:], logs[u][:, b * BANK:(b + 1) * BANK],
                                         start=True, stop=True)
                i.then_inc(mixed, 1)

            pe.wait_ge(const_in, 16 * 7)
            with pe.Fori(0, IMAGES) as n:
                group(n, aggr, x_stat, n * X_STATS + 2, x_grouped)
                pe.wait_ge(x_stat, n * X_STATS + 3)
                differences(n, 0, 0)
                differences(n, 1, 1)
                with pe.Fori(0, PAIRS - 1) as t:
                    for u in range(2):
                        differences(n, 2 * t + 2 + u, u)
                group(n, ry, y_stat, n * Y_STATS + 1, y_grouped)
                pe.wait_ge(y_stat, n * Y_STATS + 2)
                mix_channels(n, 0, 0)
                mix_channels(n, 1, 1)
                with pe.Fori(0, PAIRS - 1) as t:
                    for u in range(2):
                        mix_channels(n, 2 * t + 2 + u, u)


def kernel(x, L1_conv_exp_param, L1_conv_bias):
    import numpy as np
    import concourse.bacc as bacc
    from concourse.bass_utils import run_bass_kernel_spmd

    nc = bacc.Bacc("TRN2", target_bir_lowering=False, num_devices=1)
    part = np.arange(P)
    channel = part % (P // 2)
    eye = np.eye(P, dtype=np.float32)
    same_group = (channel[:, None] // 2 == channel[None, :] // 2).astype(np.float32) / 4
    arrays = {
        "x": np.ascontiguousarray(x),
        "exp_param": np.ascontiguousarray(L1_conv_exp_param),
        "bias": np.ascontiguousarray(L1_conv_bias),
        "eye": eye,
        "neg_eye": -eye,
        "group_mean": same_group,
    }
    aps = [nc.dram_tensor(k, a.shape, mybir.dt.from_np(a.dtype), kind="ExternalInput").ap() for k, a in arrays.items()]
    out = nc.dram_tensor("out", x.shape, F32, kind="ExternalOutput").ap()
    build(nc, *aps, out)
    r = run_bass_kernel_spmd(nc, [arrays], core_ids=[0])
    return r.results[0]["out"]
```

```python
from contextlib import ExitStack

import concourse.bass as bass
from concourse import mybir

F32 = mybir.dt.float32
ALU = mybir.AluOpType
ACT = mybir.ActivationFunctionType

P = 128
ROWS = 4
BANK = 512
STAT = 6
GN_EPS = 1e-5
SOBEL_EPS = 1e-8
LOG_SHIFT = 0.1


def build(nc, x, exp_param, bias, eye, neg_eye, group_mean, out):
    IMAGES, C, H, W = x.shape
    HALF = H // 2
    N = ROWS * W
    CH = HALF // ROWS
    PAIRS = CH // 2
    GROUP = 4
    BN = N // BANK
    BROWS = BANK // W
    LATE = 12
    LAG = 12
    EARLY = CH - LATE
    assert 2 * C == P and HALF % (2 * ROWS) == 0 and BANK % W == 0 and EARLY % 4 == 0 and LATE % GROUP == 0 and LAG >= LATE and (CH - LAG) % 4 == 0

    x_dram = x.rearrange("b c (h r) w -> b h c (r w)", h=2)
    out_dram = out.rearrange("b c (h r) w -> b h c (r w)", h=2)

    with ExitStack() as ctx:
        def sb(name, shape):
            return ctx.enter_context(nc.sbuf_tensor(name, shape, F32))

        def ps(name):
            return [ctx.enter_context(nc.psum_tensor(f"{name}{u}", [P, N], F32)) for u in range(2)]

        def sem(name):
            return ctx.enter_context(nc.semaphore(name))

        image = sb("image", [P, (HALF + 2) * W])
        pair_sum = sb("pair_sum", [P, 2, ROWS, W + 2])
        box = sb("box", [P, 2 * ROWS, W + 1])
        work = [sb(f"work{i}", [P, N])[:] for i in range(2)]
        top_box = sb("top_box", [P, 1, W + 1])
        late = sb("late", [P, LATE * N])
        plus = sb("plus", [P, P])
        minus = sb("minus", [P, P])
        grp = sb("grp", [P, P])
        mix = sb("mix", [P, P])
        bias_sb = sb("bias_sb", [P, 1])
        eps_sobel = sb("eps_sobel", [P, 1])
        eps_gn = sb("eps_gn", [P, 1])
        shift = sb("shift", [P, 1])
        bn = sb("bn", [P, CH * BN * STAT])
        aggr = sb("aggr", [P, 2])
        gx = sb("gx", [P, 2])
        sx = sb("sx", [P, 4])
        y_sum = sb("y_sum", [P, CH])
        y_sq = sb("y_sq", [P, CH])
        ry = sb("ry", [P, 2])
        my = sb("my", [P, 2])
        gy = sb("gy", [P, 2])
        sy = sb("sy", [P, 5])
        std_y = sb("std_y", [P, 1])
        scale_y = sb("scale_y", [P, 1])
        q_psum = ps("q_psum")
        g_psum = ps("g_psum")

        p_buf = logs = work
        top_pair = work[1][:, 0:W + 2].rearrange("p (r w) -> p r w", r=1)
        pair_flat = pair_sum.rearrange("p u r w -> p u (r w)")
        exps = [pair_flat[:, u, 0:N] for u in range(2)]

        const_in = sem("const_in")
        const_set = sem("const_set")
        mix_zero = sem("mix_zero")
        halo_in = sem("halo_in")
        chunk_in = [sem("chunk_in0"), sem("chunk_in1")]
        late_loaded = sem("late_loaded")
        late_in = sem("late_in")
        chunk_out = [sem("chunk_out0"), sem("chunk_out1")]
        FIRST_IN = [(EARLY // GROUP + 1) // 2 * 32, EARLY // GROUP // 2 * 32]
        PAIR_IN = EARLY // 4 * 32
        PAIR_OUT = CH // 4 * 32
        bn_done = sem("bn_done")
        x_stat = sem("x_stat")
        x_grouped = sem("x_grouped")
        padded = sem("padded")
        pairs_done = sem("pairs_done")
        top_done = sem("top_done")
        box_done = sem("box_done")
        carry_used = sem("carry_used")
        p_ready = sem("p_ready")
        q_ready = sem("q_ready")
        p_squared = sem("p_squared")
        q_squared = sem("q_squared")
        summed = sem("summed")
        rooted = sem("rooted")
        y_ready = sem("y_ready")
        y_squared = sem("y_squared")
        y_stat = sem("y_stat")
        y_grouped = sem("y_grouped")
        y_std = sem("y_std")
        clamped = sem("clamped")
        logged = sem("logged")
        mixed = sem("mixed")
        exped = sem("exped")
        final = sem("final")

        PADS = 5
        CONSTS = 7
        LATE_IN = LATE // 2 * 16
        LATE_LOADED = LATE // GROUP * 32
        X_STATS = 8
        Y_STATS = 8

        def rows(k, n=N, ahead=0):
            return image[:, bass.ds(k * N + (1 + ahead) * W, n)]

        def rows3(k, ahead=0):
            return rows(k, ahead=ahead).rearrange("p (r w) -> p r w", w=W)

        block = ctx.enter_context(nc.Block())

        @block.sync
        def _(sp):
            def load(n, k, dst, count, signal):
                for h in range(2):
                    sp.dma_start(dst[h * C:(h + 1) * C, :],
                                 x_dram[bass.ds(n, 1), h, :, bass.ds(k * N, count * N)].rearrange("b c f -> (b c) f")
                                 ).then_inc(signal, 16)

            def place(k, count=1):
                return image[:, bass.ds(k * N + W, count * N)]

            def halos(n):
                sp.dma_start(image[C:P, 0:W],
                             x_dram[bass.ds(n, 1), 0, :, (HALF - 1) * W:HALF * W].rearrange("b c f -> (b c) f")
                             ).then_inc(halo_in, 16)
                sp.dma_start(image[0:C, (HALF + 1) * W:(HALF + 2) * W],
                             x_dram[bass.ds(n, 1), 1, :, 0:W].rearrange("b c f -> (b c) f")
                             ).then_inc(halo_in, 16)

            def store(n, pair, v):
                sp.wait_ge(final, n * CH + 2 * pair + 2)
                for h in range(2):
                    sp.dma_start(out_dram[bass.ds(n, 1), h, :, bass.ds(pair * (2 * N), 2 * N)].rearrange("b c f -> (b c) f"),
                                 image[h * C:(h + 1) * C, bass.ds(pair * (2 * N) + W, 2 * N)]).then_inc(chunk_out[v], 16)

            def stored(n, quad, v):
                sp.wait_ge(chunk_out[v], n * PAIR_OUT + 32 * quad + 32)

            for g in range(EARLY // GROUP):
                if g >= 2:
                    sp.wait_ge(chunk_in[g % 2], 32 * (g // 2))
                load(0, g * GROUP, place(g * GROUP, GROUP), GROUP, chunk_in[g % 2])
            for k in range(EARLY, CH, GROUP):
                load(0, k, place(k, GROUP), GROUP, late_in)
            halos(0)
            for dst, src in ((plus[:], eye), (minus[:], neg_eye), (grp[:], group_mean)):
                sp.dma_start(dst, src).then_inc(const_in, 16)
            sp.wait_ge(mix_zero, 1)
            for h in range(2):
                sp.dma_start(mix[h * C:(h + 1) * C, h * C:(h + 1) * C],
                             exp_param.rearrange("i j a b -> i (j a b)")).then_inc(const_in, 16)
                sp.dma_start(bias_sb[h * C:(h + 1) * C, :],
                             bias.rearrange("c a b -> c (a b)")).then_inc(const_in, 16)

            with sp.Fori(0, IMAGES - 1) as n:
                sp.wait_ge(late_in, n * LATE_IN + LATE_IN)
                for g in range(LATE // GROUP):
                    load(n + 1, EARLY + g * GROUP, late[:, g * GROUP * N:(g + 1) * GROUP * N], GROUP, late_loaded)
                sp.wait_ge(pairs_done, n * CH + CH)
                halos(n + 1)
                store(n, 0, 0)
                store(n, 1, 1)
                with sp.Fori(0, EARLY // 4) as t:
                    for v in range(2):
                        pair = 2 * t + v
                        stored(n, t, v)
                        sp.wait_ge(chunk_in[v], n * PAIR_IN + (pair * 16 + FIRST_IN[v] - 16 * v))
                        load(n + 1, 2 * pair, place(2 * pair, 2), 2, chunk_in[v])
                        store(n, pair + 2, v)
                for pair in range(EARLY // 2, PAIRS):
                    stored(n, pair // 2, pair % 2)
                    sp.wait_ge(late_loaded, n * LATE_LOADED + LATE_LOADED)
                    sp.dma_start(place(2 * pair, 2), late[:, (2 * pair - EARLY) * N:(2 * pair - EARLY + 2) * N]
                                 ).then_inc(late_in, 16)
                    if pair + 2 < PAIRS:
                        store(n, pair + 2, pair % 2)
            last = IMAGES - 1
            with sp.Fori(0, PAIRS // 2) as t:
                for v in range(2):
                    store(last, 2 * t + v, v)
            for v in range(2):
                stored(last, CH // 4 - 1, v)

        @block.gpsimd
        def _(pool):
            nc.gpsimd.memset(mix[:], 0.0).then_inc(mix_zero, 1)
            for t, v in ((eps_sobel, SOBEL_EPS), (eps_gn, GN_EPS), (shift, LOG_SHIFT)):
                nc.gpsimd.memset(t[:], v).then_inc(const_set, 1)

            def pair_rows(n, k, u):
                if not (isinstance(k, int) and k < 2):
                    pool.wait_ge(box_done, n * CH + k - 1)
                nc.gpsimd.tensor_tensor(pair_sum[:, u, :, 1:W + 1], rows3(k), rows3(k, ahead=1),
                                        ALU.add).then_inc(pairs_done, 1)

            def finish(n, k, u):
                pool.wait_ge(exped, n * CH + k + 1)
                nc.gpsimd.tensor_tensor(rows(k), exps[u][:], rows(k), ALU.add).then_inc(final, 1)

            def rest_of_pairs(n):
                with pool.Fori(0, EARLY // 2 - 2) as t:
                    for u in range(2):
                        pair_rows(n, 2 * t + 2 + u, u)
                pair_rows(n, EARLY - 2, 0)
                pool.wait_ge(late_in, n * LATE_IN + LATE_IN)
                pair_rows(n, EARLY - 1, 1)
                with pool.Fori(0, LATE // 2 - 1) as t:
                    for u in range(2):
                        pair_rows(n, 2 * t + EARLY + u, u)
                pair_rows(n, CH - 2, 0)
                pool.wait_ge(padded, n * PADS + PADS)
                pool.wait_ge(halo_in, n * 32 + 32)
                pair_rows(n, CH - 1, 1)

            pool.wait_ge(bn_done, CH)
            pair_rows(0, 0, 0)
            pair_rows(0, 1, 1)
            with pool.Fori(0, IMAGES - 1) as n:
                rest_of_pairs(n)
                with pool.Fori(0, PAIRS - 1) as t:
                    for u in range(2):
                        finish(n, 2 * t + u, u)
                pool.wait_ge(bn_done, n * CH + CH + LATE + 3)
                finish(n, CH - 2, 0)
                pool.wait_ge(final, n * CH + CH - 1)
                pair_rows(n + 1, 0, 0)
                finish(n, CH - 1, 1)
                pool.wait_ge(final, n * CH + CH)
                pair_rows(n + 1, 1, 1)
            rest_of_pairs(IMAGES - 1)
            with pool.Fori(0, PAIRS) as t:
                for u in range(2):
                    finish(IMAGES - 1, 2 * t + u, u)

        @block.vector
        def _(dve):
            v = nc.vector

            def chunk_stats(k, tile, at):
                for b in range(BN):
                    i = v.bn_stats(bn[:, bass.ds(k * (BN * STAT) + b * STAT, STAT)], tile[:, bass.ds(at + b * BANK, BANK)])
                i.then_inc(bn_done, 1)

            def x_stats(n):
                s = n * X_STATS
                dve.wait_ge(bn_done, n * CH + CH)
                v.memset(sx[:, 2:3], 0.0)
                v.bn_aggr(aggr[:], bn[:]).then_inc(x_stat, 1)
                dve.wait_ge(x_stat, s + 1)
                v.scalar_tensor_tensor(out=aggr[:, 1:2], in0=aggr[:, 0:1], scalar=aggr[:, 0:1], in1=aggr[:, 1:2],
                                       op0=ALU.mult, op1=ALU.add).then_inc(x_stat, 1)
                dve.wait_ge(x_grouped, n + 1)
                v.tensor_copy(gx[:], q_psum[0][:, 0:2]).then_inc(x_stat, 1)
                dve.wait_ge(x_stat, s + 3)
                v.tensor_scalar(sx[:, 0:1], gx[:, 0:1], 2.0, None, ALU.mult).then_inc(x_stat, 1)
                v.tensor_scalar(sx[:, 1:2], gx[:, 0:1], bias_sb[:, 0:1], -1.0, ALU.add, ALU.mult)
                v.tensor_scalar(sx[:, 2:3], gx[:, 0:1], gx[:, 0:1], None, ALU.mult).then_inc(x_stat, 1)
                dve.wait_ge(x_stat, s + 5)
                v.tensor_tensor(sx[:, 2:3], gx[:, 1:2], sx[:, 2:3], ALU.subtract).then_inc(x_stat, 1)
                dve.wait_ge(x_stat, s + 6)
                v.tensor_scalar(sx[:, 3:4], sx[:, 2:3], GN_EPS, 0.5, ALU.add, ALU.mult).then_inc(x_stat, 1)
                dve.wait_ge(x_stat, s + 7)
                v.reciprocal(sx[:, 3:4], sx[:, 3:4]).then_inc(x_stat, 1)

            def top(n):
                dve.wait_ge(halo_in, n * 32 + 32)
                dve.wait_ge(padded, n * PADS + PADS)
                v.tensor_tensor(top_pair[:, 0, 1:W + 1], image[:, 0:W], image[:, W:2 * W], ALU.add).then_inc(top_done, 1)
                dve.wait_ge(top_done, 2 * n + 1)
                v.tensor_tensor(top_box[:, 0], top_pair[:, 0, 0:W + 1], top_pair[:, 0, 1:W + 2],
                                ALU.add).then_inc(top_done, 1)

            def boxes(n, k, u):
                dve.wait_ge(pairs_done, n * CH + k + 1)
                if not (isinstance(k, int) and k < 2):
                    dve.wait_ge(carry_used, n * CH + k)
                    dve.wait_ge(p_ready, n * CH + k)
                v.tensor_tensor(box[:, u * ROWS:(u + 1) * ROWS], pair_sum[:, u, :, 0:W + 1], pair_sum[:, u, :, 1:W + 2],
                                ALU.add).then_inc(box_done, 1)

            def p_difference(n, k, u):
                dve.wait_ge(box_done, n * CH + k + 1)
                if isinstance(k, int) and k == 0:
                    dve.wait_ge(top_done, 2 * n + 2)
                if not (isinstance(k, int) and k < 2):
                    dve.wait_ge(summed, n * CH + k - 1)
                dst = p_buf[u].rearrange("p (r w) -> p r w", w=W)
                if u == 0:
                    above = top_box if isinstance(k, int) and k == 0 else box[:, 2 * ROWS - 1:2 * ROWS]
                    v.tensor_tensor(dst[:, 0:1], above[:, :, 1:W + 1], box[:, 0:1, 0:W], ALU.subtract)
                    v.tensor_tensor(dst[:, 1:ROWS], box[:, 0:ROWS - 1, 1:W + 1], box[:, 1:ROWS, 0:W],
                                    ALU.subtract).then_inc(p_ready, 1)
                else:
                    v.tensor_tensor(dst, box[:, ROWS - 1:2 * ROWS - 1, 1:W + 1], box[:, ROWS:2 * ROWS, 0:W],
                                    ALU.subtract).then_inc(p_ready, 1)

            def add_squares(n, k, u):
                dve.wait_ge(q_squared, n * CH + k + 1)
                v.tensor_tensor(q_psum[u][:], q_psum[u][:], p_buf[u], ALU.add).then_inc(summed, 1)

            def add_root(n, k, u):
                dve.wait_ge(rooted, n * CH + k + 1)
                v.scalar_tensor_tensor(out=rows(k), in0=g_psum[u][:], scalar=bias_sb[:, 0:1], in1=rows(k), op0=ALU.add,
                                       op1=ALU.add, accum_out=y_sum[:, bass.ds(k, 1)]).then_inc(y_ready, 1)

            def phase_a(n):
                x_stats(n)
                top(n)
                boxes(n, 0, 0)
                p_difference(n, 0, 0)
                boxes(n, 1, 1)
                p_difference(n, 1, 1)
                add_squares(n, 0, 0)
                boxes(n, 2, 0)
                p_difference(n, 2, 0)
                add_squares(n, 1, 1)
                boxes(n, 3, 1)
                add_root(n, 0, 0)
                p_difference(n, 3, 1)
                add_squares(n, 2, 0)
                with dve.Fori(0, PAIRS - 2) as t:
                    for u in range(2):
                        k = 2 * t + 4 + u
                        boxes(n, k, u)
                        add_root(n, k - 3, 1 - u)
                        p_difference(n, k, u)
                        add_squares(n, k - 1, 1 - u)
                add_root(n, CH - 3, 1)
                add_squares(n, CH - 1, 1)
                add_root(n, CH - 2, 0)
                add_root(n, CH - 1, 1)

            def y_stats(n, between):
                s = n * Y_STATS
                dve.wait_ge(y_ready, n * CH + CH)
                v.reduce_sum(ry[:, 0:1], y_sum[:], mybir.AxisListType.X).then_inc(y_stat, 1)
                between(0)
                dve.wait_ge(y_squared, n * CH + CH)
                v.reduce_sum(ry[:, 1:2], y_sq[:], mybir.AxisListType.X).then_inc(y_stat, 1)
                dve.wait_ge(y_stat, s + 2)
                v.tensor_scalar(my[:, 0:1], ry[:, 0:1], 1.0 / (HALF * W), bias_sb[:, 0:1], ALU.mult, ALU.subtract)
                v.tensor_scalar(my[:, 1:2], ry[:, 1:2], 1.0 / (HALF * W), None, ALU.mult).then_inc(y_stat, 1)
                dve.wait_ge(y_grouped, n + 1)
                v.tensor_tensor(sy[:, 0:1], q_psum[0][:, 0:1], gx[:, 0:1], ALU.subtract).then_inc(y_stat, 1)
                v.tensor_copy(gy[:], q_psum[0][:, 0:2])
                v.tensor_scalar(sy[:, 4:5], q_psum[0][:, 0:1], bias_sb[:, 0:1], None, ALU.add).then_inc(y_stat, 1)
                dve.wait_ge(y_stat, s + 5)
                v.tensor_tensor(sy[:, 1:2], sy[:, 0:1], sy[:, 0:1], ALU.mult).then_inc(y_stat, 1)
                dve.wait_ge(y_stat, s + 6)
                v.tensor_tensor(sy[:, 2:3], gy[:, 1:2], sy[:, 1:2], ALU.subtract).then_inc(y_stat, 1)

            def y_scale(n):
                dve.wait_ge(y_std, n + 1)
                v.reciprocal(scale_y[:], std_y[:]).then_inc(y_stat, 1)

            def clamp(n, k, u):
                if not (isinstance(k, int) and k < 2):
                    dve.wait_ge(mixed, n * CH + k - 1)
                v.tensor_scalar(logs[u], rows(k), sy[:, 4:5], sy[:, 4:5], ALU.max, ALU.subtract).then_inc(clamped, 1)

            def phase_b(n, more):
                def late_stats(j):
                    if more:
                        if j == 0:
                            dve.wait_ge(late_loaded, n * LATE_LOADED + LATE_LOADED)
                        chunk_stats(EARLY + j, late, j * N)

                y_stats(n, late_stats)
                clamp(n, 0, 0)
                clamp(n, 1, 1)
                y_scale(n)
                late_stats(1)
                for k in range(2, LAG):
                    clamp(n, k, k % 2)
                    if k < LATE:
                        late_stats(k)

                def early_stats(k, quad, v, odd):
                    if not odd:
                        dve.wait_ge(chunk_in[v], n * PAIR_IN + (32 * quad + FIRST_IN[v] + 32))
                    chunk_stats(k, image, k * N + W)

                with dve.Fori(0, (CH - LAG) // 4) as t:
                    for j in range(4):
                        k = 4 * t + j
                        clamp(n, k + LAG, j % 2)
                        if more:
                            early_stats(k, t, j // 2, j % 2)
                if more:
                    for k in range(CH - LAG, EARLY):
                        early_stats(k, k // 4, k // 2 % 2, k % 2)

            for k in range(CH):
                if k % GROUP == 0 and k < EARLY:
                    dve.wait_ge(chunk_in[k // GROUP % 2], 32 * (k // GROUP // 2) + 32)
                if k == EARLY:
                    dve.wait_ge(late_in, LATE_IN)
                chunk_stats(k, image, k * N + W)
            dve.wait_ge(const_in, 16 * CONSTS)
            with dve.Fori(0, IMAGES - 1) as n:
                phase_a(n)
                phase_b(n, True)
            phase_a(IMAGES - 1)
            phase_b(IMAGES - 1, False)

        @block.scalar
        def _(act):
            a = nc.scalar

            def pad(n, first):
                act.wait_ge(x_stat, n * X_STATS + 4)
                a.copy(image[0:C, 0:W], gx[0:C, 0:1].broadcast_to([C, W])).then_inc(padded, 1)
                a.copy(image[C:P, (HALF + 1) * W:(HALF + 2) * W], gx[C:P, 0:1].broadcast_to([C, W])).then_inc(padded, 1)
                a.copy(top_pair[:, 0, 0:W + 2:W + 1], sx[:, 0:1].broadcast_to([P, 2])).then_inc(padded, 1)
                if not first:
                    act.wait_ge(final, n * CH)
                for u in range(2):
                    a.copy(pair_flat[:, u, 0:ROWS * (W + 2)].rearrange("p (r w) -> p r w", w=W + 2)[:, :, 0:W + 2:W + 1],
                           sx[:, 0:1].broadcast_to([P, 2 * ROWS]).rearrange("p (r c) -> p r c", c=2)).then_inc(padded, 1)

            def square_p(n, k, u):
                act.wait_ge(p_ready, n * CH + k + 1)
                a.activation(p_buf[u], p_buf[u], ACT.Square).then_inc(p_squared, 1)

            def square_q(n, k, u):
                act.wait_ge(q_ready, n * CH + k + 1)
                a.activation(q_psum[u][:], q_psum[u][:], ACT.Square).then_inc(q_squared, 1)

            def root(n, k, u):
                act.wait_ge(summed, n * CH + k + 1)
                if not (isinstance(k, int) and k < 2):
                    act.wait_ge(y_squared, n * CH + k - 1)
                a.activation(g_psum[u][:], q_psum[u][:], ACT.Sqrt, bias=eps_sobel[:, 0:1],
                             scale=sx[:, 3:4]).then_inc(rooted, 1)

            def square_y(n, k, u):
                act.wait_ge(y_ready, n * CH + k + 1)
                a.activation(g_psum[u][:], rows(k), ACT.Square, bias=sx[:, 1:2],
                             accum_out=y_sq[:, bass.ds(k, 1)]).then_inc(y_squared, 1)

            def phase_a(n, first=False):
                a.preload_act_table_set("sqrt_and_others")
                pad(n, first)
                square_p(n, 0, 0)
                square_q(n, 0, 0)
                act.wait_ge(x_stat, n * X_STATS + X_STATS)
                root(n, 0, 0)
                square_p(n, 1, 1)
                square_q(n, 1, 1)
                root(n, 1, 1)
                for k in (2, 3):
                    square_p(n, k, k % 2)
                    square_q(n, k, k % 2)
                    square_y(n, k - 2, k % 2)
                    root(n, k, k % 2)
                with act.Fori(0, PAIRS - 2) as t:
                    for u in range(2):
                        k = 2 * t + 4 + u
                        square_p(n, k, u)
                        square_q(n, k, u)
                        square_y(n, k - 2, u)
                        root(n, k, u)
                square_y(n, CH - 2, 0)
                square_y(n, CH - 1, 1)
                act.wait_ge(y_stat, n * Y_STATS + 7)
                a.activation(std_y[:], sy[:, 2:3], ACT.Sqrt, bias=eps_gn[:, 0:1]).then_inc(y_std, 1)

            def log(n, k, u):
                act.wait_ge(clamped, n * CH + k + 1)
                a.activation(logs[u], logs[u], ACT.Ln, bias=shift[:, 0:1], scale=scale_y[:, 0:1]).then_inc(logged, 1)

            def exp(n, k, u):
                act.wait_ge(mixed, n * CH + k + 1)
                if not (isinstance(k, int) and k < 2):
                    act.wait_ge(final, n * CH + k - 1)
                a.activation(exps[u], g_psum[u][:], ACT.Exp).then_inc(exped, 1)

            def phase_b(n):
                a.preload_act_table_set("natural_log_exp_and_others")
                act.wait_ge(y_stat, n * Y_STATS + Y_STATS)
                log(n, 0, 0)
                log(n, 1, 1)
                exp(n, 0, 0)
                log(n, 2, 0)
                exp(n, 1, 1)
                log(n, 3, 1)
                exp(n, 2, 0)
                with act.Fori(0, PAIRS - 2) as t:
                    for u in range(2):
                        k = 2 * t + 4 + u
                        log(n, k, u)
                        exp(n, k - 1, 1 - u)
                exp(n, CH - 1, 1)

            act.wait_ge(const_set, 3)
            phase_a(0, True)
            phase_b(0)
            with act.Fori(1, IMAGES) as n:
                phase_a(n)
                phase_b(n)

        @block.tensor
        def _(pe):
            def q_difference(n, k, u):
                pe.wait_ge(box_done, n * CH + k + 1)
                if isinstance(k, int) and k == 0:
                    pe.wait_ge(top_done, 2 * n + 2)
                if not (isinstance(k, int) and k < 2):
                    pe.wait_ge(rooted, n * CH + k - 1)
                for bank in range(BN):
                    dst = q_psum[u][:, bank * BANK:(bank + 1) * BANK]
                    r = u * ROWS + bank * BROWS
                    nc.tensor.matmul(dst, plus[:], box[:, r:r + BROWS, 1:W + 1], start=True, stop=False)
                    if r == 0:
                        above = top_box[:, 0] if isinstance(k, int) and k == 0 else box[:, 2 * ROWS - 1]
                        nc.tensor.matmul(dst[:, 0:W], minus[:], above[:, 0:W], start=False, stop=False)
                        i = nc.tensor.matmul(dst[:, W:BANK], minus[:], box[:, 0:BROWS - 1, 0:W], start=False, stop=True)
                    else:
                        i = nc.tensor.matmul(dst, minus[:], box[:, r - 1:r - 1 + BROWS, 0:W], start=False, stop=True)
                    if bank == 0:
                        i.then_inc(carry_used, 1)
                i.then_inc(q_ready, 1)

            def group(src, signal):
                nc.tensor.matmul(q_psum[0][:, 0:2], grp[:], src[:], start=True, stop=True).then_inc(signal, 1)

            def mix_channels(n, k, u):
                pe.wait_ge(logged, n * CH + k + 1)
                if not (isinstance(k, int) and k < 2):
                    pe.wait_ge(exped, n * CH + k - 1)
                for b in range(BN):
                    i = nc.tensor.matmul(g_psum[u][:, b * BANK:(b + 1) * BANK], mix[:], logs[u][:, b * BANK:(b + 1) * BANK],
                                         start=True, stop=True)
                i.then_inc(mixed, 1)

            pe.wait_ge(const_in, 16 * CONSTS)
            with pe.Fori(0, IMAGES) as n:
                pe.wait_ge(x_stat, n * X_STATS + 2)
                group(aggr, x_grouped)
                q_difference(n, 0, 0)
                q_difference(n, 1, 1)
                with pe.Fori(0, PAIRS - 1) as t:
                    for u in range(2):
                        q_difference(n, 2 * t + 2 + u, u)
                pe.wait_ge(y_stat, n * Y_STATS + 3)
                group(my, y_grouped)
                mix_channels(n, 0, 0)
                mix_channels(n, 1, 1)
                with pe.Fori(0, PAIRS - 1) as t:
                    for u in range(2):
                        mix_channels(n, 2 * t + 2 + u, u)


def kernel(x, L1_conv_exp_param, L1_conv_bias):
    import numpy as np
    import concourse.bacc as bacc
    from concourse.bass_utils import run_bass_kernel_spmd

    nc = bacc.Bacc("TRN2", target_bir_lowering=False, num_devices=1)
    part = np.arange(P)
    channel = part % (P // 2)
    eye = np.eye(P, dtype=np.float32)
    same_group = (channel[:, None] // 2 == channel[None, :] // 2).astype(np.float32) / 4
    arrays = {
        "x": np.ascontiguousarray(x),
        "exp_param": np.ascontiguousarray(L1_conv_exp_param),
        "bias": np.ascontiguousarray(L1_conv_bias),
        "eye": eye,
        "neg_eye": -eye,
        "group_mean": same_group,
    }
    aps = [nc.dram_tensor(k, a.shape, mybir.dt.from_np(a.dtype), kind="ExternalInput").ap() for k, a in arrays.items()]
    out = nc.dram_tensor("out", x.shape, F32, kind="ExternalOutput").ap()
    build(nc, *aps, out)
    r = run_bass_kernel_spmd(nc, [arrays], core_ids=[0])
    return r.results[0]["out"]
```

```python
from contextlib import ExitStack

import concourse.bass as bass
from concourse import mybir

F32 = mybir.dt.float32
ALU = mybir.AluOpType
ACT = mybir.ActivationFunctionType

P = 128
ROWS = 4
BANK = 512
STAT = 6
GN_EPS = 1e-5
SOBEL_EPS = 1e-8
LOG_SHIFT = 0.1


def build(nc, x, exp_param, bias, eye, neg_eye, group_mean, out):
    IMAGES, C, H, W = x.shape
    HALF = H // 2
    N = ROWS * W
    CH = HALF // ROWS
    PAIRS = CH // 2
    GROUP = 4
    BN = N // BANK
    BROWS = BANK // W
    LATE = 12
    EARLY = CH - LATE
    BOXED = EARLY - 2
    LAG = LATE + 2
    SHARE = 192
    REST = N - SHARE
    WARM_A, WARM_Y, WARM_B = 2, 5, 3
    assert 2 * C == P and HALF % (2 * ROWS) == 0 and BANK % W == 0 and EARLY % 4 == 0 and LATE % GROUP == 0
    assert (CH - LAG - 2) % 4 == 0 and BN == 2

    x_dram = x.rearrange("b c (h r) w -> b h c (r w)", h=2)
    out_dram = out.rearrange("b c (h r) w -> b h c (r w)", h=2)

    with ExitStack() as ctx:
        def sb(name, shape):
            return ctx.enter_context(nc.sbuf_tensor(name, shape, F32))

        def ps(name):
            return [ctx.enter_context(nc.psum_tensor(f"{name}{u}", [P, N], F32)) for u in range(4)]

        def sem(name):
            return ctx.enter_context(nc.semaphore(name))

        image = sb("image", [P, (HALF + 2) * W])
        pair_sum = sb("pair_sum", [P, 2, ROWS, W + 2])
        box = sb("box", [P, 2 * ROWS, W + 1])
        work = [sb(f"work{i}", [P, N])[:] for i in range(2)]
        top_box = sb("top_box", [P, 1, W + 1])
        late = sb("late", [P, LATE * N])
        plus = sb("plus", [P, P])
        minus = sb("minus", [P, P])
        grp = sb("grp", [P, P])
        mix = sb("mix", [P, P])
        bias_sb = sb("bias_sb", [P, 1])
        eps_sobel = sb("eps_sobel", [P, 1])
        eps_gn = sb("eps_gn", [P, 1])
        shift = sb("shift", [P, 1])
        bn = sb("bn", [P, CH * BN * STAT])
        aggr = sb("aggr", [P, 2])
        gx = sb("gx", [P, 2])
        sx = sb("sx", [P, 4])
        y_sum = sb("y_sum", [P, CH])
        y_sq = sb("y_sq", [P, CH])
        ry = sb("ry", [P, 2])
        my = sb("my", [P, 2])
        gy = sb("gy", [P, 2])
        sy = sb("sy", [P, 5])
        log_var = sb("log_var", [P, 1])
        scale_y = sb("scale_y", [P, 1])
        psum = ps("psum")
        mix_psum = psum[2:]

        p_buf = logs = work
        top_pair = work[1][:, 0:W + 2].rearrange("p (r w) -> p r w", r=1)
        box_flat = box.rearrange("p r w -> p (r w)")
        pair_flat = pair_sum.rearrange("p u r w -> p u (r w)")
        exps = [pair_flat[:, u, 0:N] for u in range(2)]

        const_in = sem("const_in")
        const_set = sem("const_set")
        mix_zero = sem("mix_zero")
        halo_in = sem("halo_in")
        chunk_in = [sem("chunk_in0"), sem("chunk_in1")]
        late_loaded = sem("late_loaded")
        late_in = sem("late_in")
        boxed_loaded = sem("boxed_loaded")
        boxed_in = sem("boxed_in")
        chunk_out = [sem("chunk_out0"), sem("chunk_out1")]
        FIRST_IN = [(EARLY // GROUP + 1) // 2 * 32, EARLY // GROUP // 2 * 32]
        PAIR_IN = [EARLY // 4 * 32, (EARLY // 4 - 1) * 32]
        PAIR_OUT = CH // 4 * 32
        bn_done = sem("bn_done")
        x_stat = sem("x_stat")
        x_grouped = sem("x_grouped")
        padded = sem("padded")
        pairs_done = sem("pairs_done")
        top_done = sem("top_done")
        box_done = sem("box_done")
        carry_used = sem("carry_used")
        p_ready = sem("p_ready")
        q_ready = sem("q_ready")
        pool_squared = sem("pool_squared")
        q_squared = sem("q_squared")
        summed = sem("summed")
        pe_summed = sem("pe_summed")
        rooted = sem("rooted")
        y_ready = sem("y_ready")
        y_squared = sem("y_squared")
        y_stat = sem("y_stat")
        y_grouped = sem("y_grouped")
        y_scaled = sem("y_scaled")
        clamped = sem("clamped")
        logged = sem("logged")
        mixed = sem("mixed")
        exped = sem("exped")
        final = sem("final")
        dve_final = sem("dve_final")

        PADS = 5
        CONSTS = 7
        LATE_IN = LATE // 2 * 16
        LATE_LOADED = LATE // GROUP * 32
        PE_SUMS = CH - 1
        X_STATS = 8
        Y_STATS = 7

        def rows(k, n=N, ahead=0):
            return image[:, bass.ds(k * N + (1 + ahead) * W, n)]

        def rows3(k, ahead=0):
            return rows(k, ahead=ahead).rearrange("p (r w) -> p r w", w=W)

        def first_loads():
            late = [(k, late_in, 8 * (k - EARLY)) for k in range(EARLY, CH, GROUP)]
            early = [(k, chunk_in[k // GROUP % 2], 32 * (k // GROUP // 2)) for k in range(0, EARLY, GROUP)]
            order = []
            while early or late:
                order.append(late.pop(0) if late and len(early) <= 2 * len(late) - 2 or not early else early.pop(0))
            return order

        block = ctx.enter_context(nc.Block())

        @block.sync
        def _(sp):
            def load(n, k, dst, count, signal):
                for h in range(2):
                    sp.dma_start(dst[h * C:(h + 1) * C, :],
                                 x_dram[bass.ds(n, 1), h, :, bass.ds(k * N, count * N)].rearrange("b c f -> (b c) f")
                                 ).then_inc(signal, 16)

            def place(k, count=1):
                return image[:, bass.ds(k * N + W, count * N)]

            def halos(n):
                sp.dma_start(image[C:P, 0:W],
                             x_dram[bass.ds(n, 1), 0, :, (HALF - 1) * W:HALF * W].rearrange("b c f -> (b c) f")
                             ).then_inc(halo_in, 16)
                sp.dma_start(image[0:C, (HALF + 1) * W:(HALF + 2) * W],
                             x_dram[bass.ds(n, 1), 1, :, 0:W].rearrange("b c f -> (b c) f")
                             ).then_inc(halo_in, 16)

            def store(n, pair, v):
                sp.wait_ge(final, n * CH + 2 * pair + 2)
                sp.wait_ge(dve_final, n * CH + 2 * pair + 2)
                for h in range(2):
                    sp.dma_start(out_dram[bass.ds(n, 1), h, :, bass.ds(pair * (2 * N), 2 * N)].rearrange("b c f -> (b c) f"),
                                 image[h * C:(h + 1) * C, bass.ds(pair * (2 * N) + W, 2 * N)]).then_inc(chunk_out[v], 16)

            def stored(n, quad, v):
                sp.wait_ge(chunk_out[v], n * PAIR_OUT + 32 * quad + 32)

            for k, signal, landed in first_loads():
                if landed > 0:
                    sp.wait_ge(signal, landed)
                load(0, k, place(k, GROUP), GROUP, signal)
            halos(0)
            for dst, src in ((plus[:], eye), (minus[:], neg_eye), (grp[:], group_mean)):
                sp.dma_start(dst, src).then_inc(const_in, 16)
            sp.wait_ge(mix_zero, 1)
            for h in range(2):
                sp.dma_start(mix[h * C:(h + 1) * C, h * C:(h + 1) * C],
                             exp_param.rearrange("i j a b -> i (j a b)")).then_inc(const_in, 16)
                sp.dma_start(bias_sb[h * C:(h + 1) * C, :],
                             bias.rearrange("c a b -> c (a b)")).then_inc(const_in, 16)

            with sp.Fori(0, IMAGES - 1) as n:
                sp.wait_ge(late_in, n * LATE_IN + LATE_IN)
                for g in range(LATE // GROUP):
                    load(n + 1, EARLY + g * GROUP, late[:, g * GROUP * N:(g + 1) * GROUP * N], GROUP, late_loaded)
                sp.wait_ge(pairs_done, n * CH + CH)
                halos(n + 1)
                sp.wait_ge(q_ready, n * CH + CH)
                sp.wait_ge(p_ready, n * CH + CH)
                load(n + 1, BOXED, box_flat[:, 0:2 * N], 2, boxed_loaded)
                store(n, 0, 0)
                store(n, 1, 1)

                def replace(pair, quad, v):
                    stored(n, quad, v)
                    sp.wait_ge(chunk_in[v], n * PAIR_IN[v] + (32 * quad + FIRST_IN[v]))
                    load(n + 1, 2 * pair, place(2 * pair, 2), 2, chunk_in[v])
                    store(n, pair + 2, v)

                with sp.Fori(0, EARLY // 4 - 1) as t:
                    for v in range(2):
                        replace(2 * t + v, t, v)
                replace(EARLY // 2 - 2, EARLY // 4 - 1, 0)
                stored(n, EARLY // 4 - 1, 1)
                sp.wait_ge(boxed_loaded, n * 32 + 32)
                sp.dma_start(place(BOXED, 2), box_flat[:, 0:2 * N]).then_inc(boxed_in, 16)
                store(n, EARLY // 2 + 1, 1)
                for pair in range(EARLY // 2, PAIRS):
                    stored(n, pair // 2, pair % 2)
                    sp.wait_ge(late_loaded, n * LATE_LOADED + LATE_LOADED)
                    sp.dma_start(place(2 * pair, 2), late[:, (2 * pair - EARLY) * N:(2 * pair - EARLY + 2) * N]
                                 ).then_inc(late_in, 16)
                    if pair + 2 < PAIRS:
                        store(n, pair + 2, pair % 2)
            last = IMAGES - 1
            with sp.Fori(0, PAIRS // 2) as t:
                for v in range(2):
                    store(last, 2 * t + v, v)
            for v in range(2):
                stored(last, CH // 4 - 1, v)

        @block.gpsimd
        def _(pool):
            nc.gpsimd.memset(mix[:], 0.0).then_inc(mix_zero, 1)
            for t, v in ((eps_sobel, SOBEL_EPS), (eps_gn, GN_EPS), (shift, LOG_SHIFT)):
                nc.gpsimd.memset(t[:], v).then_inc(const_set, 1)

            def pair_rows(n, k, u):
                if not (isinstance(k, int) and k < 2):
                    pool.wait_ge(box_done, n * CH + k - 1)
                nc.gpsimd.tensor_tensor(pair_sum[:, u, :, 1:W + 1], rows3(k), rows3(k, ahead=1),
                                        ALU.add).then_inc(pairs_done, 1)

            def finish(n, k, u):
                pool.wait_ge(exped, n * CH + k + 1)
                nc.gpsimd.tensor_tensor(rows(k, REST), exps[u][:, 0:REST], rows(k, REST), ALU.add).then_inc(final, 1)

            def rest_of_pairs(n):
                with pool.Fori(0, EARLY // 2 - 2) as t:
                    for u in range(2):
                        pair_rows(n, 2 * t + 2 + u, u)
                pair_rows(n, EARLY - 2, 0)
                pool.wait_ge(late_in, n * LATE_IN + LATE_IN)
                pair_rows(n, EARLY - 1, 1)
                with pool.Fori(0, LATE // 2 - 1) as t:
                    for u in range(2):
                        pair_rows(n, 2 * t + EARLY + u, u)
                pair_rows(n, CH - 2, 0)
                pool.wait_ge(padded, n * PADS + PADS)
                pool.wait_ge(halo_in, n * 32 + 32)
                pair_rows(n, CH - 1, 1)
                for k in range(CH - 2, CH):
                    pool.wait_ge(p_ready, n * CH + k + 1)
                    nc.gpsimd.tensor_tensor(p_buf[k % 2], p_buf[k % 2], p_buf[k % 2], ALU.mult).then_inc(pool_squared, 1)

            pool.wait_ge(bn_done, CH)
            pair_rows(0, 0, 0)
            pair_rows(0, 1, 1)
            with pool.Fori(0, IMAGES - 1) as n:
                rest_of_pairs(n)
                with pool.Fori(0, PAIRS - 1) as t:
                    for u in range(2):
                        finish(n, 2 * t + u, u)
                pool.wait_ge(bn_done, n * CH + CH + LAG + 3)
                finish(n, CH - 2, 0)
                pool.wait_ge(final, n * CH + CH - 1)
                pool.wait_ge(dve_final, n * CH + CH - 1)
                pair_rows(n + 1, 0, 0)
                finish(n, CH - 1, 1)
                pool.wait_ge(final, n * CH + CH)
                pool.wait_ge(dve_final, n * CH + CH)
                pair_rows(n + 1, 1, 1)
            rest_of_pairs(IMAGES - 1)
            with pool.Fori(0, PAIRS) as t:
                for u in range(2):
                    finish(IMAGES - 1, 2 * t + u, u)

        @block.vector
        def _(dve):
            v = nc.vector

            def chunk_stats(k, tile, at):
                for b in range(BN):
                    i = v.bn_stats(bn[:, bass.ds(k * (BN * STAT) + b * STAT, STAT)], tile[:, bass.ds(at + b * BANK, BANK)])
                i.then_inc(bn_done, 1)

            def x_aggregate(n):
                s = n * X_STATS
                dve.wait_ge(bn_done, n * CH + CH)
                v.memset(sx[:, 2:3], 0.0)
                v.bn_aggr(aggr[:], bn[:]).then_inc(x_stat, 1)
                dve.wait_ge(x_stat, s + 1)
                v.scalar_tensor_tensor(out=aggr[:, 1:2], in0=aggr[:, 0:1], scalar=aggr[:, 0:1], in1=aggr[:, 1:2],
                                       op0=ALU.mult, op1=ALU.add).then_inc(x_stat, 1)

            def x_group(n):
                s = n * X_STATS
                dve.wait_ge(x_grouped, n + 1)
                v.tensor_copy(gx[:], psum[0][:, 0:2]).then_inc(x_stat, 1)
                dve.wait_ge(x_stat, s + 3)
                v.tensor_scalar(sx[:, 0:1], gx[:, 0:1], 2.0, None, ALU.mult).then_inc(x_stat, 1)
                v.tensor_scalar(sx[:, 1:2], gx[:, 0:1], bias_sb[:, 0:1], -1.0, ALU.add, ALU.mult)
                v.tensor_scalar(sx[:, 2:3], gx[:, 0:1], gx[:, 0:1], None, ALU.mult).then_inc(x_stat, 1)
                dve.wait_ge(x_stat, s + 5)
                v.tensor_tensor(sx[:, 2:3], gx[:, 1:2], sx[:, 2:3], ALU.subtract).then_inc(x_stat, 1)
                dve.wait_ge(x_stat, s + 6)
                v.tensor_scalar(sx[:, 3:4], sx[:, 2:3], GN_EPS, 0.5, ALU.add, ALU.mult).then_inc(x_stat, 1)
                dve.wait_ge(x_stat, s + 7)
                v.reciprocal(sx[:, 3:4], sx[:, 3:4]).then_inc(x_stat, 1)

            def top(n):
                dve.wait_ge(halo_in, n * 32 + 32)
                dve.wait_ge(padded, n * PADS + PADS - 1)
                v.tensor_tensor(top_pair[:, 0, 1:W + 1], image[:, 0:W], image[:, W:2 * W], ALU.add).then_inc(top_done, 1)
                dve.wait_ge(top_done, 2 * n + 1)
                v.tensor_tensor(top_box[:, 0], top_pair[:, 0, 0:W + 1], top_pair[:, 0, 1:W + 2],
                                ALU.add).then_inc(top_done, 1)

            def boxes(n, k, u):
                dve.wait_ge(pairs_done, n * CH + k + 1)
                if isinstance(k, int) and k < 2:
                    dve.wait_ge(padded, n * PADS + PADS - 1 + k)
                if not (isinstance(k, int) and k < 2):
                    dve.wait_ge(carry_used, n * CH + k)
                    dve.wait_ge(p_ready, n * CH + k)
                v.tensor_tensor(box[:, u * ROWS:(u + 1) * ROWS], pair_sum[:, u, :, 0:W + 1], pair_sum[:, u, :, 1:W + 2],
                                ALU.add).then_inc(box_done, 1)

            def p_difference(n, k, u):
                dve.wait_ge(box_done, n * CH + k + 1)
                if isinstance(k, int) and k == 0:
                    dve.wait_ge(top_done, 2 * n + 2)
                if not (isinstance(k, int) and k < 2):
                    dve.wait_ge(summed, n * CH + k - 1)
                    dve.wait_ge(pe_summed, n * PE_SUMS + k - 1)
                dst = p_buf[u].rearrange("p (r w) -> p r w", w=W)
                if u == 0:
                    above = top_box if isinstance(k, int) and k == 0 else box[:, 2 * ROWS - 1:2 * ROWS]
                    v.tensor_tensor(dst[:, 0:1], above[:, :, 1:W + 1], box[:, 0:1, 0:W], ALU.subtract)
                    v.tensor_tensor(dst[:, 1:ROWS], box[:, 0:ROWS - 1, 1:W + 1], box[:, 1:ROWS, 0:W],
                                    ALU.subtract).then_inc(p_ready, 1)
                else:
                    v.tensor_tensor(dst, box[:, ROWS - 1:2 * ROWS - 1, 1:W + 1], box[:, ROWS:2 * ROWS, 0:W],
                                    ALU.subtract).then_inc(p_ready, 1)

            def add_squares(n, k, z, columns=BANK):
                if isinstance(k, int) and k >= CH - 2:
                    dve.wait_ge(pool_squared, n * 2 + k - CH + 3)
                dve.wait_ge(q_squared, n * CH + k + 1)
                v.tensor_tensor(psum[z][:, 0:columns], psum[z][:, 0:columns], p_buf[z % 2][:, 0:columns],
                                ALU.add).then_inc(summed, 1)

            def add_root(n, k, z):
                dve.wait_ge(rooted, n * CH + k + 1)
                v.scalar_tensor_tensor(out=rows(k), in0=psum[z][:], scalar=bias_sb[:, 0:1], in1=rows(k), op0=ALU.add,
                                       op1=ALU.add, accum_out=y_sum[:, bass.ds(k, 1)]).then_inc(y_ready, 1)

            def phase_a(n):
                for k in range(4):
                    boxes(n, k, k % 2)
                    if k == 0:
                        top(n)
                    if k == 3:
                        add_root(n, 0, 0)
                    p_difference(n, k, k % 2)
                    if k > 0:
                        add_squares(n, k - 1, k - 1)

                def step(k, j, columns=BANK):
                    boxes(n, k, j % 2)
                    add_root(n, k - 3, (j + 1) % 4)
                    p_difference(n, k, j % 2)
                    add_squares(n, k - 1, (j + 3) % 4, columns)

                with dve.Fori(0, CH // 4 - 2) as t:
                    for j in range(4):
                        step(4 * t + 4 + j, j)
                for j in range(4):
                    step(CH - 4 + j, j, N if j == 3 else BANK)
                add_root(n, CH - 3, 1)
                add_squares(n, CH - 1, 3)
                add_root(n, CH - 2, 2)
                add_root(n, CH - 1, 3)

            def y_stats(n, meanwhile):
                s = n * Y_STATS
                dve.wait_ge(y_ready, n * CH + CH)
                v.reduce_sum(ry[:, 0:1], y_sum[:], mybir.AxisListType.X).then_inc(y_stat, 1)
                meanwhile(0)
                dve.wait_ge(y_squared, n * CH + CH)
                v.reduce_sum(ry[:, 1:2], y_sq[:], mybir.AxisListType.X).then_inc(y_stat, 1)
                dve.wait_ge(y_stat, s + 2)
                v.tensor_scalar(my[:, 0:1], ry[:, 0:1], 1.0 / (HALF * W), bias_sb[:, 0:1], ALU.mult, ALU.subtract)
                v.tensor_scalar(my[:, 1:2], ry[:, 1:2], 1.0 / (HALF * W), None, ALU.mult).then_inc(y_stat, 1)
                dve.wait_ge(y_grouped, n + 1)
                v.tensor_tensor(sy[:, 0:1], psum[0][:, 0:1], gx[:, 0:1], ALU.subtract).then_inc(y_stat, 1)
                v.tensor_copy(gy[:], psum[0][:, 0:2])
                v.tensor_scalar(sy[:, 4:5], psum[0][:, 0:1], bias_sb[:, 0:1], None, ALU.add).then_inc(y_stat, 1)
                dve.wait_ge(y_stat, s + 5)
                v.tensor_tensor(sy[:, 1:2], sy[:, 0:1], sy[:, 0:1], ALU.mult).then_inc(y_stat, 1)
                dve.wait_ge(y_stat, s + 6)
                v.tensor_tensor(sy[:, 2:3], gy[:, 1:2], sy[:, 1:2], ALU.subtract).then_inc(y_stat, 1)

            def clamp(n, k, u):
                if not (isinstance(k, int) and k < 2):
                    dve.wait_ge(mixed, n * CH + k - 1)
                v.tensor_scalar(logs[u], rows(k), sy[:, 4:5], sy[:, 4:5], ALU.max, ALU.subtract).then_inc(clamped, 1)

            def finish_share(n, k, u):
                dve.wait_ge(exped, n * CH + k + 1)
                v.tensor_tensor(rows(k, N)[:, REST:N], exps[u][:, REST:N], rows(k, N)[:, REST:N], ALU.add).then_inc(dve_final, 1)

            def phase_b(n, more):
                def late_stats(j):
                    if more:
                        if j == 0:
                            dve.wait_ge(late_loaded, n * LATE_LOADED + LATE_LOADED)
                        if j == LATE:
                            dve.wait_ge(boxed_loaded, n * 32 + 32)
                        if j < LATE:
                            chunk_stats(EARLY + j, late, j * N)
                        else:
                            chunk_stats(BOXED + j - LATE, box_flat, (j - LATE) * N)

                y_stats(n, late_stats)
                clamp(n, 0, 0)
                clamp(n, 1, 1)
                late_stats(1)
                for k in range(2, LAG):
                    clamp(n, k, k % 2)
                    late_stats(k)
                    finish_share(n, k - 2, k % 2)

                def early_stats(k, quad, v, odd):
                    if more:
                        if not odd:
                            dve.wait_ge(chunk_in[v], n * PAIR_IN[v] + (32 * quad + FIRST_IN[v] + 32))
                        chunk_stats(k, image, k * N + W)

                with dve.Fori(0, (CH - LAG - 2) // 4) as t:
                    for j in range(4):
                        clamp(n, 4 * t + j + LAG, j % 2)
                        early_stats(4 * t + j, t, j // 2, j % 2)
                        finish_share(n, 4 * t + j + LAG - 2, j % 2)
                for k in range(CH - 2, CH):
                    clamp(n, k, k % 2)
                    finish_share(n, k - 2, k % 2)
                early_stats(CH - 2 - LAG, (CH - 2 - LAG) // 4, (CH - 2 - LAG) // 2 % 2, 0)
                finish_share(n, CH - 2, 0)
                early_stats(CH - 1 - LAG, (CH - 1 - LAG) // 4, (CH - 1 - LAG) // 2 % 2, 1)
                if more:
                    x_aggregate(n + 1)
                finish_share(n, CH - 1, 1)
                if more:
                    x_group(n + 1)
                    dve.wait_ge(boxed_in, n * 16 + 16)

            for first, signal, landed in first_loads():
                dve.wait_ge(signal, landed + 32)
                for k in range(first, first + GROUP):
                    chunk_stats(k, image, k * N + W)
            dve.wait_ge(const_in, 16 * CONSTS)
            x_aggregate(0)
            x_group(0)
            with dve.Fori(0, IMAGES - 1) as n:
                phase_a(n)
                phase_b(n, True)
            phase_a(IMAGES - 1)
            phase_b(IMAGES - 1, False)

        @block.scalar
        def _(act):
            a = nc.scalar

            def pad(n, first):
                act.wait_ge(x_stat, n * X_STATS + 4)
                a.copy(image[0:C, 0:W], gx[0:C, 0:1].broadcast_to([C, W])).then_inc(padded, 1)
                a.copy(image[C:P, (HALF + 1) * W:(HALF + 2) * W], gx[C:P, 0:1].broadcast_to([C, W])).then_inc(padded, 1)
                a.copy(top_pair[:, 0, 0:W + 2:W + 1], sx[:, 0:1].broadcast_to([P, 2])).then_inc(padded, 1)
                for u in range(2):
                    if not first:
                        act.wait_ge(final, n * CH - 1 + u)
                        act.wait_ge(dve_final, n * CH - 1 + u)
                    a.copy(pair_flat[:, u, 0:ROWS * (W + 2)].rearrange("p (r w) -> p r w", w=W + 2)[:, :, 0:W + 2:W + 1],
                           sx[:, 0:1].broadcast_to([P, 2 * ROWS]).rearrange("p (r c) -> p r c", c=2)).then_inc(padded, 1)
                    if u == 0:
                        a.preload_act_table_set("sqrt_and_others")

            def square_p(n, k, u):
                act.wait_ge(p_ready, n * CH + k + 1)
                a.activation(p_buf[u], p_buf[u], ACT.Square)

            def square_q(n, k, z):
                act.wait_ge(q_ready, n * CH + k + 1)
                a.activation(psum[z][:], psum[z][:], ACT.Square).then_inc(q_squared, 1)

            def root(n, k, z):
                act.wait_ge(summed, n * CH + k + 1)
                if not (isinstance(k, int) and k == CH - 2):
                    act.wait_ge(pe_summed, n * PE_SUMS + (PE_SUMS if isinstance(k, int) and k == CH - 1 else k + 1))
                a.activation(psum[z][:], psum[z][:], ACT.Sqrt, bias=eps_sobel[:, 0:1], scale=sx[:, 3:4]).then_inc(rooted, 1)

            def square_y(n, k, z):
                act.wait_ge(y_ready, n * CH + k + 1)
                a.activation(psum[z][:], rows(k), ACT.Square, bias=sx[:, 1:2],
                             accum_out=y_sq[:, bass.ds(k, 1)]).then_inc(y_squared, 1)

            def phase_a(n, first=False):
                pad(n, first)
                for k in range(4):
                    square_p(n, k, k % 2)
                    square_q(n, k, k)
                    if k == 1:
                        act.wait_ge(x_stat, n * X_STATS + X_STATS)
                    if k > 0:
                        root(n, k - 1, k - 1)
                square_y(n, 0, 0)

                def step(k, j):
                    if not (isinstance(k, int) and k >= CH - 2):
                        square_p(n, k, j % 2)
                    square_y(n, k - 3, (j + 1) % 4)
                    if isinstance(k, int) and k == CH - 1:
                        root(n, k - 1, (j + 3) % 4)
                        square_q(n, k, j)
                    else:
                        square_q(n, k, j)
                        root(n, k - 1, (j + 3) % 4)

                with act.Fori(0, CH // 4 - 2) as t:
                    for j in range(4):
                        step(4 * t + 4 + j, j)
                for j in range(4):
                    step(CH - 4 + j, j)
                square_y(n, CH - 3, 1)
                root(n, CH - 1, 3)
                square_y(n, CH - 2, 2)
                square_y(n, CH - 1, 3)

            def log(n, k, u):
                act.wait_ge(clamped, n * CH + k + 1)
                a.activation(logs[u], logs[u], ACT.Ln, bias=shift[:, 0:1], scale=scale_y[:, 0:1]).then_inc(logged, 1)

            def exp(n, k, u):
                act.wait_ge(mixed, n * CH + k + 1)
                if not (isinstance(k, int) and k < 2):
                    act.wait_ge(final, n * CH + k - 1)
                    act.wait_ge(dve_final, n * CH + k - 1)
                a.activation(exps[u], mix_psum[u][:], ACT.Exp).then_inc(exped, 1)

            def phase_b(n):
                a.preload_act_table_set("natural_log_exp_and_others")
                act.wait_ge(y_stat, n * Y_STATS + Y_STATS)
                a.activation(log_var[:], sy[:, 2:3], ACT.Ln, bias=eps_gn[:, 0:1]).then_inc(y_scaled, 1)
                act.wait_ge(y_scaled, 2 * n + 1)
                a.activation(scale_y[:], log_var[:], ACT.Exp, scale=-0.5).then_inc(y_scaled, 1)
                act.wait_ge(y_scaled, 2 * n + 2)
                log(n, 0, 0)
                log(n, 1, 1)
                exp(n, 0, 0)
                log(n, 2, 0)
                exp(n, 1, 1)
                log(n, 3, 1)
                exp(n, 2, 0)
                with act.Fori(0, PAIRS - 2) as t:
                    for u in range(2):
                        k = 2 * t + 4 + u
                        log(n, k, u)
                        exp(n, k - 1, 1 - u)
                exp(n, CH - 1, 1)

            act.wait_ge(const_set, 3)
            phase_a(0, True)
            phase_b(0)
            with act.Fori(1, IMAGES) as n:
                phase_a(n)
                phase_b(n)

        @block.tensor
        def _(pe):
            def q_difference(n, k, z):
                pe.wait_ge(box_done, n * CH + k + 1)
                if not (isinstance(k, int) and k < 4):
                    pe.wait_ge(y_squared, n * CH + k - 3)
                for bank in range(BN):
                    dst = psum[z][:, bank * BANK:(bank + 1) * BANK]
                    r = z % 2 * ROWS + bank * BROWS
                    nc.tensor.matmul(dst, plus[:], box[:, r:r + BROWS, 1:W + 1], start=True, stop=False)
                    if r == 0:
                        nc.tensor.matmul(dst[:, W:BANK], minus[:], box[:, 0:BROWS - 1, 0:W], start=False, stop=False)
                        above = box[:, 2 * ROWS - 1]
                        if isinstance(k, int) and k == 0:
                            pe.wait_ge(top_done, 2 * n + 2)
                            above = top_box[:, 0]
                        i = nc.tensor.matmul(dst[:, 0:W], minus[:], above[:, 0:W], start=False, stop=True)
                    else:
                        i = nc.tensor.matmul(dst, minus[:], box[:, r - 1:r - 1 + BROWS, 0:W], start=False, stop=True)
                    if bank == 0:
                        i.then_inc(carry_used, 1)
                i.then_inc(q_ready, 1)

            def sum_squares(n, k, z):
                pe.wait_ge(q_squared, n * CH + k + 1)
                if isinstance(k, int) and k == CH - 1:
                    pe.wait_ge(pool_squared, n * 2 + 2)
                for bank in range(1, BN):
                    columns = slice(bank * BANK, (bank + 1) * BANK)
                    i = nc.tensor.matmul(psum[z][:, columns], plus[:], p_buf[z % 2][:, columns], start=False, stop=True,
                                         skip_group_check=True)
                i.then_inc(pe_summed, 1)

            def warm(count, z):
                for _ in range(count):
                    nc.tensor.matmul(psum[z][:, 0:BANK], plus[:], image[:, W:W + BANK], start=True, stop=True)

            def group(src, signal):
                nc.tensor.matmul(psum[0][:, 0:2], grp[:], src[:], start=True, stop=True).then_inc(signal, 1)

            def mix_channels(n, k, u):
                pe.wait_ge(logged, n * CH + k + 1)
                if not (isinstance(k, int) and k < 2):
                    pe.wait_ge(exped, n * CH + k - 1)
                for b in range(BN):
                    i = nc.tensor.matmul(mix_psum[u][:, b * BANK:(b + 1) * BANK], mix[:], logs[u][:, b * BANK:(b + 1) * BANK],
                                         start=True, stop=True)
                i.then_inc(mixed, 1)

            pe.wait_ge(const_in, 16 * CONSTS)
            with pe.Fori(0, IMAGES) as n:
                pe.wait_ge(x_stat, n * X_STATS + 2)
                group(aggr, x_grouped)
                warm(WARM_A, 1)
                q_difference(n, 0, 0)
                for k in range(1, 4):
                    q_difference(n, k, k)
                    sum_squares(n, k - 1, k - 1)
                with pe.Fori(0, CH // 4 - 2) as t:
                    for j in range(4):
                        k = 4 * t + 4 + j
                        q_difference(n, k, j)
                        sum_squares(n, k - 1, (j + 3) % 4)
                for k in range(CH - 4, CH):
                    q_difference(n, k, k % 4)
                    if k < CH - 1:
                        sum_squares(n, k - 1, (k - 1) % 4)
                sum_squares(n, CH - 1, 3)
                pe.wait_ge(y_squared, n * CH + CH - 3)
                warm(WARM_Y, 0)
                pe.wait_ge(y_stat, n * Y_STATS + 3)
                group(my, y_grouped)
                warm(WARM_B, 1)
                mix_channels(n, 0, 0)
                mix_channels(n, 1, 1)
                with pe.Fori(0, PAIRS - 1) as t:
                    for u in range(2):
                        mix_channels(n, 2 * t + 2 + u, u)


def kernel(x, L1_conv_exp_param, L1_conv_bias):
    import numpy as np
    import concourse.bacc as bacc
    from concourse.bass_utils import run_bass_kernel_spmd

    nc = bacc.Bacc("TRN2", target_bir_lowering=False, num_devices=1)
    part = np.arange(P)
    channel = part % (P // 2)
    eye = np.eye(P, dtype=np.float32)
    same_group = (channel[:, None] // 2 == channel[None, :] // 2).astype(np.float32) / 4
    arrays = {
        "x": np.ascontiguousarray(x),
        "exp_param": np.ascontiguousarray(L1_conv_exp_param),
        "bias": np.ascontiguousarray(L1_conv_bias),
        "eye": eye,
        "neg_eye": -eye,
        "group_mean": same_group,
    }
    aps = [nc.dram_tensor(k, a.shape, mybir.dt.from_np(a.dtype), kind="ExternalInput").ap() for k, a in arrays.items()]
    out = nc.dram_tensor("out", x.shape, F32, kind="ExternalOutput").ap()
    build(nc, *aps, out)
    r = run_bass_kernel_spmd(nc, [arrays], core_ids=[0])
    return r.results[0]["out"]
```
